# Optimizing a Trainium2 kernel written in Bass

```python
import numpy as np
import jax
import jax.numpy as jnp

def _softmax(x, axis=-1):
    return jax.nn.softmax(x, axis=axis)

def _gelu(x):
    return jax.nn.gelu(x, approximate=True)

def _silu(x):
    return jax.nn.silu(x)

def _sigmoid(x):
    return jax.nn.sigmoid(x)

def _layernorm(x, axis=-1, eps=1e-05):
    m = jnp.mean(x, axis=axis, keepdims=True)
    v = jnp.var(x, axis=axis, keepdims=True)
    return (x - m) / jnp.sqrt(v + eps)

def _scatter_add(tgt, idx, src, axis=0):
    return tgt.at[idx].add(src)

def _segment_sum(src, seg, n):
    return jax.ops.segment_sum(src, seg, n)
kernel_name = 'mk_adaln_ffn_d1_seqx_r4_26e5df'

def setup_inputs(seed: int=0):
    np.random.seed(seed)
    _w = jnp.asarray

    def _rec_inputs():
        import jax
        import jax.numpy as jnp
        _rk = jax.random.key(seed)
        x = -7.109e-05 + 0.9999 * jax.random.normal(jax.random.fold_in(_rk, 1), (128, 64, 1024), jnp.float32)
        _lenS = 64 - jax.random.randint(jax.random.fold_in(_rk, 7), (128,), 0, max(1, 64 // 4) + 1, jnp.int32)
        _lenS2 = 64 - jax.random.randint(jax.random.fold_in(_rk, 8), (128,), 0, max(1, 64 // 4) + 1, jnp.int32)
        itok_B_0_15 = jax.random.randint(jax.random.fold_in(_rk, 11), (128,), 0, 16, jnp.int32)
        return (x, itok_B_0_15)
    x, itok_B_0_15 = _rec_inputs()

    def _L0_cond_setup():
        import jax, jax.numpy as jnp
        import numpy as np
        B, C, T = (64, 64, 1024)
        S, D = (16, 64)
        key = jax.random.key(seed)
        k1, k2, k3 = jax.random.split(key, 3)
        x = jax.random.normal(k1, (B, C, T), dtype=jnp.float32)
        condition = jax.random.randint(k2, (B,), 0, S, dtype=jnp.int64)
        bound = float(np.sqrt(6.0 / C))
        weights = jax.random.uniform(k3, (S, C, D), dtype=jnp.float32, minval=-bound, maxval=bound)
        return {'x': x, 'condition': condition, 'weights': weights}
    _L0_cond_all = _L0_cond_setup()
    _L0_cond_in = {k: v for k, v in _L0_cond_all.items() if k in ('weights',)}
    del _L0_cond_all

    def _L0_ffn_setup():
        import jax, jax.numpy as jnp
        import numpy as np
        BATCH, TOK, DIM, OUT = (4, 512, 1024, 1024)
        E, R, TOP_K = (8, 16, 2)
        SCALING = 16.0 / R
        key = jax.random.key(seed)
        ks = jax.random.split(key, 6)
        return {'x': jax.random.normal(ks[0], (BATCH, TOK, DIM), dtype=jnp.float32), 'W_base': jax.random.normal(ks[1], (OUT, DIM), dtype=jnp.float32) / np.sqrt(DIM), 'b_base': jax.random.normal(ks[2], (OUT,), dtype=jnp.float32) * 0.01, 'W_gate': jax.random.normal(ks[3], (E, DIM), dtype=jnp.float32) * 0.01, 'A': jax.random.normal(ks[4], (E, R, DIM), dtype=jnp.float32) / np.sqrt(DIM), 'B': jax.random.normal(ks[5], (OUT, OUT // OUT * R * 0 + R), dtype=jnp.float32)[None].repeat(E, 0) * 0.0 + jax.random.normal(ks[5], (E, OUT, R), dtype=jnp.float32) * 0.02}
    _L0_ffn_all = _L0_ffn_setup()
    _L0_ffn_in = {k: v for k, v in _L0_ffn_all.items() if k in ('W_base', 'b_base', 'W_gate', 'A', 'B')}
    del _L0_ffn_all
    return {'x': x, 'itok_B_0_15': itok_B_0_15, 'L0_cond_weights': _L0_cond_in['weights'], 'L0_ffn_W_base': _L0_ffn_in['W_base'], 'L0_ffn_b_base': _L0_ffn_in['b_base'], 'L0_ffn_W_gate': _L0_ffn_in['W_gate'], 'L0_ffn_A': _L0_ffn_in['A'], 'L0_ffn_B': _L0_ffn_in['B']}

def reference(x, itok_B_0_15, L0_cond_weights, L0_ffn_W_base, L0_ffn_b_base, L0_ffn_W_gate, L0_ffn_A, L0_ffn_B):
    import jax
    import jax.numpy as jnp

    def _L0_cond_ref(x, condition, weights):
        import jax, jax.numpy as jnp
        import numpy as np
        B, C, T = (64, 64, 1024)
        S, D = (16, 64)
        W = weights[condition]
        return jnp.einsum('bct,bcd->bdt', x, W)

    def _L0_ffn_ref(x, W_base, b_base, W_gate, A, B):
        import jax, jax.numpy as jnp
        import numpy as np
        BATCH, TOK, DIM, OUT = (4, 512, 1024, 1024)
        E, R, TOP_K = (8, 16, 2)
        SCALING = 16.0 / R
        result = jnp.einsum('bnd,od->bno', x, W_base) + b_base
        logits = jnp.einsum('bnd,ed->bne', x, W_gate)
        probs = jax.nn.softmax(logits.astype(jnp.float32), axis=-1)
        top_p, top_i = jax.lax.top_k(probs, TOP_K)
        top_p = top_p / jnp.sum(top_p, axis=-1, keepdims=True)
        top_p = top_p.astype(x.dtype)
        route_w = jnp.sum(jax.nn.one_hot(top_i, E, dtype=x.dtype) * top_p[..., None], axis=-2)
        h = jnp.einsum('bnd,erd->bner', x, A)
        hw = h * route_w[..., None]
        delta = jnp.einsum('bner,eor->bno', hw, B)
        return result + delta * SCALING
    x = x + _L0_ffn_ref(_L0_cond_ref(x, itok_B_0_15, L0_cond_weights), L0_ffn_W_base, L0_ffn_b_base, L0_ffn_W_gate, L0_ffn_A, L0_ffn_B)
    return x

_drawn_inputs = setup_inputs


def setup_inputs(seed=0):
    import zlib

    import numpy as np

    out = dict(_drawn_inputs(seed))
    spreads = {}
    factors = {'L0_ffn_b_base': 8.0}
    for name, (base, spread) in spreads.items():
        noise = np.random.default_rng([zlib.crc32(name.encode()), seed]).standard_normal(out[name].shape)
        drawn = base * np.exp(spread * noise) if base else spread * noise
        out[name] = jnp.asarray(drawn.astype(out[name].dtype))
    for name, factor in factors.items():
        out[name] = (out[name] * factor).astype(out[name].dtype)
    return out
```

```python
from contextlib import ExitStack

import concourse.bass as bass
from concourse import mybir

F32 = mybir.dt.float32
F32R = mybir.dt.float32r
I32 = mybir.dt.int32
U32 = mybir.dt.uint32
ALU = mybir.AluOpType
ACT = mybir.ActivationFunctionType

P = 128
BANK = 512


def adaln_ffn(nc, x, cond, cond_w, w_base_t, gate_a_t, b_t, b_base, out):
    ROWS, T = x.shape
    S, C, D = cond_w.shape
    O = w_base_t.shape[1]
    ER = b_t.shape[0]
    HG = gate_a_t.shape[1]
    E = HG - ER
    R = ER // E
    TILES = ROWS // P
    KT = T // P
    HALVES = O // BANK
    KH = KT // 2
    PAIRS = TILES // 2
    assert C == D == P // 2 and ER == P and T == 2 * BANK and O == 2 * BANK and E == 8

    with ExitStack() as ctx:
        def sb(name, shape, dt=F32):
            return ctx.enter_context(nc.sbuf_tensor(name, shape, dt))

        def psum(name, shape):
            return ctx.enter_context(nc.psum_tensor(name, shape, F32))

        def sem(name):
            return ctx.enter_context(nc.semaphore(name))

        cond_sb = sb("cond_sb", [1, cond.shape[1]], I32)
        table = sb("table", [P, S, D])
        w_raw = sb("w_raw", [P, KT, O])
        w_hi = sb("w_hi", [P, KT, O], F32R)
        w_lo = sb("w_lo", [P, KT, O], F32R)
        ga_raw = sb("ga_raw", [P, KT, HG])
        ga = sb("ga", [P, KT, 2 * HG], F32R)
        b_raw = sb("b_raw", [P, O])
        b_hi = sb("b_hi", [P, O], F32R)
        b_lo = sb("b_lo", [P, O], F32R)
        bias = sb("bias", [P, O])
        ident = sb("ident", [P, P])
        expert = sb("expert", [P, E])

        x_sb = [sb(f"x_sb{s}", [P, T]) for s in range(2)]
        mix = [sb(f"mix{s}", [P, P]) for s in range(2)]
        y_hi = [sb(f"y_hi{s}", [P, KT, P], F32R) for s in range(2)]
        y_lo = [sb(f"y_lo{s}", [P, KT, P], F32R) for s in range(2)]
        o_sb = [sb(f"o_sb{s}", [P, O]) for s in range(2)]

        hg_part = sb("hg_part", [P, HG])
        hg = sb("hg", [P, HG])
        top = sb("top", [P, 8])
        top_at = sb("top_at", [P, 8], U32)
        top_atf = sb("top_atf", [P, 2])
        neg_top = sb("neg_top", [P, 1])
        e2 = sb("e2", [P, 2])
        e_sum = sb("e_sum", [P, 1])
        e_inv = sb("e_inv", [P, 1])
        w2 = sb("w2", [P, 2])
        pick = sb("pick", [P, 2, E])
        route = sb("route", [P, E])
        hw = sb("hw", [P, ER])
        hwt_hi = sb("hwt_hi", [P, P], F32R)
        hwt_lo = sb("hwt_lo", [P, P], F32R)

        ps_y = [psum(f"ps_y{h}", [P, KH, P]) for h in range(2)]
        ps_out = [[psum(f"ps_out{s}{n}", [P, BANK]) for n in range(HALVES)] for s in range(2)]
        ps_hg = psum("ps_hg", [P, BANK])
        ps_hwt = psum("ps_hwt", [P, BANK])

        s_cond_in = sem("cond_in")
        s_table_in = sem("table_in")
        s_ga_in = sem("ga_in")
        s_b_in = sem("b_in")
        s_bias_in = sem("bias_in")
        s_w_in = [sem(f"w_in{k}") for k in range(KT)]
        s_x_in = [sem(f"x_in{s}") for s in range(2)]
        s_mix_clear = sem("mix_clear")
        s_ident = sem("ident_made")
        s_iota = sem("iota_made")
        s_ga_hi = sem("ga_hi_made")
        s_ga_lo = sem("ga_lo_made")
        s_w_hi = sem("w_hi_made")
        s_w_lo = sem("w_lo_made")
        s_b_hi = sem("b_hi_made")
        s_b_lo = sem("b_lo_made")
        s_mix = sem("mix_ready")
        s_yt = sem("yt_ready")
        s_y_hi = sem("y_hi_ready")
        s_y_lo = sem("y_lo_ready")
        s_hg_mm = sem("hg_summed")
        s_hg_part = sem("hg_part_copied")
        s_logits = sem("logits_ready")
        s_hg = sem("h_ready")
        s_top = sem("top_ready")
        s_top_at = sem("top_at_ready")
        s_top_atf = sem("top_atf_ready")
        s_neg_top = sem("neg_top_ready")
        s_e = sem("exp_ready")
        s_e_inv = sem("e_inv_ready")
        s_w2 = sem("w2_ready")
        s_pick = sem("pick_ready")
        s_route = sem("route_ready")
        s_hw = sem("hw_ready")
        s_hwt = sem("hwt_ready")
        s_hwt_hi = sem("hwt_hi_ready")
        s_hwt_lo = sem("hwt_lo_ready")
        s_out_mm = sem("out_summed")
        s_res = sem("residual_ready")
        s_out = sem("out_ready")
        s_stored = [sem(f"stored{s}") for s in range(2)]

        def pairs(engine, body):
            for slot in range(2):
                body(0, slot)
            with engine.Fori(1, PAIRS - 1) as g:
                for slot in range(2):
                    body(g, slot)
            for slot in range(2):
                body(PAIRS - 1, slot)

        def first_pair(g):
            return isinstance(g, int) and g == 0

        def first(g, slot):
            return first_pair(g) and slot == 0

        def last(g, slot):
            return isinstance(g, int) and g == PAIRS - 1 and slot == 1

        block = ctx.enter_context(nc.Block())

        @block.sync
        def _(sp):
            sp.dma_start(x_sb[0][:], x[0:P, :]).then_inc(s_x_in[0], 16)
            for k in range(KT):
                sp.dma_start(w_raw[:, k, :], w_base_t[k * P:(k + 1) * P, :]).then_inc(s_w_in[k], 16)
                if k == 1:
                    sp.dma_start(x_sb[1][:], x[P:2 * P, :]).then_inc(s_x_in[1], 16)

            def store(i, slot):
                row = i * P
                sp.wait_ge(s_out, 2 * i + 2)
                sp.dma_start(out[bass.ds(row, P), :], o_sb[slot][:]).then_inc(s_stored[slot], 16)

            def load(i, slot):
                row = i * P
                sp.wait_ge(s_res, i - 1)
                sp.wait_ge(s_yt, 2 * i - 2)
                sp.dma_start(x_sb[slot][:], x[bass.ds(row, P), :]).then_inc(s_x_in[slot], 16)

            load(2, 0)
            load(3, 1)
            store(0, 0)
            with sp.Fori(1, PAIRS - 1) as g:
                load(g * 2 + 2, 0)
                store(g * 2 - 1, 1)
                load(g * 2 + 3, 1)
                store(g * 2, 0)
            store(TILES - 3, 1)
            store(TILES - 2, 0)
            store(TILES - 1, 1)
            for slot in range(2):
                sp.wait_ge(s_stored[slot], 16 * PAIRS)

        @block.gpsimd
        def _(pool):
            for slot in range(2):
                pool.memset(mix[slot][:], 0.0).then_inc(s_mix_clear, 1)
            pool.memset(ident[:], 0.0).then_inc(s_mix_clear, 1)
            pool.iota(expert[:], [[1, E]], base=0, channel_multiplier=0,
                      allow_small_or_imprecise_dtypes=True).then_inc(s_iota, 1)
            pool.wait_ge(s_mix_clear, 3)
            pool.affine_select(out=ident[:], in_=ident[:], compare_op=ALU.not_equal, fill=1.0, base=0,
                               pattern=[[-1, P]], channel_multiplier=1).then_inc(s_ident, 1)
            pool.wait_ge(s_cond_in, 16)
            pool.wait_ge(s_table_in, 32)

            def tile(g, slot):
                i = g * 2 + slot
                c = [pool.value_load(cond_sb[0:1, bass.ds(i * 2 + b, 1)], min_val=0, max_val=S - 1)
                     for b in range(2)]
                if not first_pair(g):
                    pool.wait_ge(s_yt, 2 * i - 2)
                if first(g, slot):
                    pool.wait_ge(s_ident, 1)
                else:
                    pool.wait_ge(s_res, i)
                for b in range(2):
                    part = slice(b * C, (b + 1) * C)
                    if b == 1:
                        pool.wait_ge(s_mix, 2 * i + 1)
                    pool.tensor_copy(mix[slot][part, b * D:(b + 1) * D].unsqueeze(1),
                                     table[part, bass.ds(c[b], 1), :]).then_inc(s_mix, 1)
                pool.wait_ge(s_mix, 2 * i + 2)
                pool.wait_ge(s_x_in[slot], (g + 1) * 16)
                if first(g, slot):
                    pool.wait_ge(s_bias_in, 16)
                if not first_pair(g):
                    pool.wait_ge(s_stored[slot], g * 16)
                pool.tensor_tensor(o_sb[slot][:], x_sb[slot][:], bias[:], ALU.add).then_inc(s_res, 1)

            pairs(pool, tile)

        @block.scalar
        def _(act):
            act.dma_start(cond_sb[:], cond).then_inc(s_cond_in, 16)
            for b in range(2):
                act.dma_start(table[b * C:(b + 1) * C], cond_w.rearrange("s c d -> c s d")).then_inc(s_table_in, 16)
            act.dma_start(ga_raw[:], gate_a_t.rearrange("(k p) n -> p k n", p=P)).then_inc(s_ga_in, 16)
            act.dma_start(bias[:], b_base.to_broadcast([P, O])).then_inc(s_bias_in, 16)
            act.dma_start(b_raw[:], b_t).then_inc(s_b_in, 16)

            def y_parts(i, slot, fresh=False):
                if not fresh:
                    act.wait_ge(s_out_mm, i - 1)
                for h in range(2):
                    act.wait_ge(s_yt, 2 * i + h + 1)
                    act.copy(y_hi[slot][:, h * KH:(h + 1) * KH, :], ps_y[h][:]).then_inc(s_y_hi, 1)

            y_parts(0, 0, fresh=True)
            act.wait_ge(s_ga_in, 16)
            act.copy(ga[:, :, 0:HG], ga_raw[:]).then_inc(s_ga_hi, 1)
            for k in range(KT):
                act.wait_ge(s_w_in[k], 16)
                act.copy(w_hi[:, k, :], w_raw[:, k, :]).then_inc(s_w_hi, 1)
            act.wait_ge(s_b_in, 16)
            act.copy(b_hi[:], b_raw[:]).then_inc(s_b_hi, 1)

            def tile(g, slot):
                i = g * 2 + slot
                act.wait_ge(s_hg_mm, i + 1)
                act.copy(hg_part[:], ps_hg[:, HG:2 * HG]).then_inc(s_hg_part, 1)
                act.wait_ge(s_neg_top, i + 1)
                act.activation(e2[:], top[:, 0:2], ACT.Exp, bias=neg_top[:], accum_out=e_sum[:]).then_inc(s_e, 1)
                if not last(g, slot):
                    y_parts(i + 1, 1 - slot, fresh=first(g, slot))
                act.wait_ge(s_hwt, i + 1)
                act.copy(hwt_hi[:], ps_hwt[:, 0:P]).then_inc(s_hwt_hi, 1)

            pairs(act, tile)

        @block.vector
        def _(dve):
            def y_rest(i, slot):
                for h in range(2):
                    dve.wait_ge(s_y_hi, 2 * i + h + 1)
                    part = slice(h * KH, (h + 1) * KH)
                    dve.tensor_tensor(y_lo[slot][:, part, :], ps_y[h][:], y_hi[slot][:, part, :].bitcast(F32),
                                      ALU.subtract).then_inc(s_y_lo, 1)

            y_rest(0, 0)
            dve.wait_ge(s_ga_hi, 1)
            dve.tensor_tensor(ga[:, :, HG:2 * HG], ga_raw[:], ga[:, :, 0:HG].bitcast(F32),
                              ALU.subtract).then_inc(s_ga_lo, 1)
            for k in range(KT):
                dve.wait_ge(s_w_hi, k + 1)
                dve.tensor_tensor(w_lo[:, k, :], w_raw[:, k, :], w_hi[:, k, :].bitcast(F32),
                                  ALU.subtract).then_inc(s_w_lo, 1)
            dve.wait_ge(s_b_hi, 1)
            dve.tensor_tensor(b_lo[:], b_raw[:], b_hi[:].bitcast(F32), ALU.subtract).then_inc(s_b_lo, 1)
            dve.wait_ge(s_iota, 1)

            def tile(g, slot):
                i = g * 2 + slot
                dve.wait_ge(s_hg_part, i + 1)
                logits = hg[:, ER:HG]
                dve.tensor_tensor(logits, ps_hg[:, ER:HG], hg_part[:, ER:HG], ALU.add).then_inc(s_logits, 1)
                dve.wait_ge(s_logits, i + 1)
                dve.tensor_tensor(hg[:, 0:ER], ps_hg[:, 0:ER], hg_part[:, 0:ER], ALU.add).then_inc(s_hg, 1)
                dve.max(top[:], logits).then_inc(s_top, 1)
                dve.wait_ge(s_top, i + 1)
                dve.tensor_scalar(neg_top[:], top[:, 0:1], -1.0, None, ALU.mult).then_inc(s_neg_top, 1)
                dve.max_index(top_at[:], top[:], logits).then_inc(s_top_at, 1)
                dve.wait_ge(s_top_at, i + 1)
                dve.tensor_copy(top_atf[:], top_at[:, 0:2]).then_inc(s_top_atf, 1)
                dve.wait_ge(s_e, i + 1)
                dve.reciprocal(e_inv[:], e_sum[:]).then_inc(s_e_inv, 1)
                dve.wait_ge(s_e_inv, i + 1)
                dve.tensor_scalar(w2[:], e2[:], e_inv[:], None, ALU.mult).then_inc(s_w2, 1)
                dve.wait_ge(s_top_atf, i + 1)
                dve.wait_ge(s_w2, i + 1)
                for j in range(2):
                    dve.tensor_scalar(pick[:, j, :], expert[:], top_atf[:, j:j + 1], w2[:, j:j + 1],
                                      ALU.is_equal, ALU.mult).then_inc(s_pick, 1)
                dve.wait_ge(s_pick, 2 * i + 2)
                dve.tensor_tensor(route[:], pick[:, 0, :], pick[:, 1, :], ALU.add).then_inc(s_route, 1)
                dve.wait_ge(s_hg, i + 1)
                dve.wait_ge(s_route, i + 1)
                dve.tensor_tensor(hw[:].rearrange("p (e r) -> p e r", e=E),
                                  hg[:, 0:ER].rearrange("p (e r) -> p e r", e=E),
                                  route[:].unsqueeze(2).to_broadcast([P, E, R]), ALU.mult).then_inc(s_hw, 1)
                if not last(g, slot):
                    y_rest(i + 1, 1 - slot)
                dve.wait_ge(s_hwt_hi, i + 1)
                dve.tensor_tensor(hwt_lo[:], ps_hwt[:, 0:P], hwt_hi[:].bitcast(F32),
                                  ALU.subtract).then_inc(s_hwt_lo, 1)
                dve.wait_ge(s_res, i + 1)
                dve.wait_ge(s_out_mm, i + 1)
                for n in range(HALVES):
                    half = slice(n * BANK, (n + 1) * BANK)
                    dve.tensor_tensor(o_sb[slot][:, half], ps_out[slot][n][:], o_sb[slot][:, half],
                                      ALU.add).then_inc(s_out, 1)

            pairs(dve, tile)

        @block.tensor
        def _(pe):
            def stage1(i, slot, loads, fresh=False):
                pe.wait_ge(s_x_in[slot], loads * 16)
                pe.wait_ge(s_mix, 2 * i + 2)
                for k in range(KT):
                    h, kk = divmod(k, KH)
                    if kk == 0 and not fresh:
                        pe.wait_ge(s_y_lo, 2 * i + h - 1)
                    mm = pe.matmul(ps_y[h][:, kk, :], x_sb[slot][:, k * P:(k + 1) * P], mix[slot][:],
                                   start=(kk == 0), stop=(kk == KH - 1), skip_group_check=True)
                    if kk == KH - 1:
                        mm.then_inc(s_yt, 1)

            def gate(g, slot):
                i = g * 2 + slot
                if first(g, slot):
                    pe.wait_ge(s_ga_lo, 1)
                else:
                    pe.wait_ge(s_hg, i)
                for k in range(KT):
                    if k % KH == 0:
                        pe.wait_ge(s_y_lo, 2 * i + k // KH + 1)
                    for part in (y_hi, y_lo):
                        mm = pe.matmul(ps_hg[:, 0:2 * HG], part[slot][:, k, :], ga[:, k, :],
                                       start=(k == 0 and part is y_hi), stop=(k == KT - 1 and part is y_lo))
                mm.then_inc(s_hg_mm, 1)

            def base(g, slot, ks):
                for k in ks:
                    if first(g, slot):
                        pe.wait_ge(s_w_lo, k + 1)
                    for y, w in ((y_hi, w_hi), (y_hi, w_lo), (y_lo, w_hi)):
                        for n in range(HALVES):
                            pe.matmul(ps_out[slot][n][:], y[slot][:, k, :], w[:, k, n * BANK:(n + 1) * BANK],
                                      start=(k == 0 and y is y_hi and w is w_hi), stop=False)

            def turn_hw(g, slot):
                i = g * 2 + slot
                if first(g, slot):
                    pe.wait_ge(s_ident, 1)
                else:
                    pe.wait_ge(s_hwt_lo, i)
                pe.wait_ge(s_hw, i + 1)
                pe.transpose(ps_hwt[:, 0:P], hw[:], ident[:]).then_inc(s_hwt, 1)

            def lora(g, slot):
                i = g * 2 + slot
                if first(g, slot):
                    pe.wait_ge(s_b_lo, 1)
                pe.wait_ge(s_hwt_lo, i + 1)
                for q, (h, b) in enumerate(((hwt_hi, b_hi), (hwt_hi, b_lo), (hwt_lo, b_hi))):
                    for n in range(HALVES):
                        mm = pe.matmul(ps_out[slot][n][:], h[:], b[:, n * BANK:(n + 1) * BANK],
                                       start=False, stop=(q == 2))
                mm.then_inc(s_out_mm, 1)

            def tile(g, slot):
                i = g * 2 + slot
                gate(g, slot)
                if not first_pair(g):
                    pe.wait_ge(s_out, 2 * i - 2)
                base(g, slot, range(KH))
                if not last(g, slot):
                    stage1(i + 1, 1 - slot, g + slot + 1)
                base(g, slot, range(KH, KT - 2))
                turn_hw(g, slot)
                base(g, slot, range(KT - 2, KT))
                lora(g, slot)

            stage1(0, 0, 1, fresh=True)
            pairs(pe, tile)


def kernel(x, itok_B_0_15, L0_cond_weights, L0_ffn_W_base, L0_ffn_b_base, L0_ffn_W_gate, L0_ffn_A, L0_ffn_B):
    import numpy as np
    import concourse.bacc as bacc
    from concourse.bass_utils import run_bass_kernel_spmd

    batches, channels, t = x.shape
    experts, rank, _ = L0_ffn_A.shape
    o = L0_ffn_W_base.shape[0]
    arrays = {
        "x": np.reshape(x, (batches * channels, t)),
        "cond": np.reshape(itok_B_0_15, (1, batches)),
        "cond_w": L0_cond_weights,
        "w_base_t": np.transpose(L0_ffn_W_base),
        "gate_a_t": np.transpose(np.concatenate([np.reshape(L0_ffn_A, (experts * rank, t)), L0_ffn_W_gate])),
        "b_t": np.reshape(np.transpose(L0_ffn_B, (0, 2, 1)), (experts * rank, o)),
        "b_base": np.reshape(L0_ffn_b_base, (1, o)),
    }
    nc = bacc.Bacc("TRN2", target_bir_lowering=False, num_devices=1)
    ins, args = {}, []
    for name, a in arrays.items():
        a = np.ascontiguousarray(a)
        ins[f"in_{name}"] = a
        args.append(nc.dram_tensor(f"in_{name}", a.shape, mybir.dt.from_np(a.dtype), kind="ExternalInput").ap())
    out = nc.dram_tensor("out_x", (batches * channels, o), F32, kind="ExternalOutput").ap()
    adaln_ffn(nc, *args, out)
    r = run_bass_kernel_spmd(nc, [ins], core_ids=[0])
    return np.reshape(r.results[0]["out_x"], (batches, channels, o))
```

```python
from contextlib import ExitStack

import concourse.bass as bass
from concourse import mybir

F32 = mybir.dt.float32
F32R = mybir.dt.float32r
I32 = mybir.dt.int32
U32 = mybir.dt.uint32
BF16 = mybir.dt.bfloat16
ALU = mybir.AluOpType
ACT = mybir.ActivationFunctionType

P = 128
BANK = 512
BASE_COLS = [256, 384, 384]
PIECE = [1, 2, 2]
WARM_UP = 10


def adaln_ffn(nc, x, x_t, cond, cond_w, w_t, b_t, b_base, out):
    ROWS, T = x.shape
    C, S, D = cond_w.shape
    ER, O = b_t.shape
    COLS = w_t.shape[1]
    HG = COLS - O
    E = HG - ER
    R = ER // E
    TILES = ROWS // P
    KT = T // P
    PAIRS = TILES // 2
    CHUNKS = len(BASE_COLS)
    KH = KT // 2
    PIECES = [KT // n for n in PIECE]
    pieces_before = [sum(PIECES[:c]) for c in range(CHUNKS)]
    width = [n + HG * (c == 0) for c, n in enumerate(BASE_COLS)]
    at = [sum(width[:c]) for c in range(CHUNKS)]
    base_at = [sum(BASE_COLS[:c]) for c in range(CHUNKS)]
    H_AT = BASE_COLS[0]
    L_AT = H_AT + ER
    assert C == D == P // 2 and ER == P and E == 8 and sum(BASE_COLS) == O and max(width) <= BANK

    with ExitStack() as ctx:
        def sb(name, shape, dt=F32):
            return ctx.enter_context(nc.sbuf_tensor(name, shape, dt))

        def psum(name):
            return ctx.enter_context(nc.psum_tensor(name, [P, BANK], F32))

        def sem(name):
            return ctx.enter_context(nc.semaphore(name))

        cond_sb = sb("cond_sb", [1, cond.shape[1]], I32)
        table_raw = sb("table_raw", [P, S, D])
        table = sb("table", [P, S, 2, D], F32R)
        w_raw = sb("w_raw", [P, KT, COLS])
        w_hi = sb("w_hi", [P, KT, COLS], F32R)
        w_lo = sb("w_lo", [P, KT, COLS], F32R)
        b_raw = sb("b_raw", [P, O])
        b_hi = sb("b_hi", [P, O], F32R)
        b_lo = sb("b_lo", [P, O], F32R)
        bias = sb("bias", [P, O])
        ident = sb("ident", [P, P])
        expert = sb("expert", [P, E])

        xt_sb = [sb(f"xt_sb{s}", [P, KT, P]) for s in range(2)]
        x_hi = [sb(f"x_hi{s}", [P, KT, P], F32R) for s in range(2)]
        x_lo = [sb(f"x_lo{s}", [P, KT, P], F32R) for s in range(2)]
        mix = [sb(f"mix{s}", [P, 2, P], F32R) for s in range(2)]
        o_sb = [sb(f"o_sb{s}", [P, O]) for s in range(2)]

        z_hi = sb("z_hi", [P, COLS], F32R)
        z_lo = sb("z_lo", [P, COLS], F32R)
        h_sb = sb("h_sb", [P, ER])
        top = sb("top", [P, 8])
        top_at = sb("top_at", [P, 8], U32)
        top_atf = sb("top_atf", [P, 2])
        neg_top = sb("neg_top", [P, 1])
        one = sb("one", [P, 2])
        zeros = sb("zeros", [P, BANK], BF16)
        e2 = sb("e2", [P, 2])
        e_sum = sb("e_sum", [P, 1])
        e_inv = sb("e_inv", [P, 1])
        w2 = sb("w2", [P, 2])
        pick = sb("pick", [P, 2, E])
        route = sb("route", [P, E])
        hw = sb("hw", [P, ER])
        hwt_hi = sb("hwt_hi", [P, P], F32R)
        hwt_lo = sb("hwt_lo", [P, P], F32R)

        ps_z = [psum(f"ps_z{c}") for c in range(CHUNKS + 1)]
        ps_out = [psum(f"ps_out{c}") for c in range(CHUNKS)]
        ps_hwt = psum("ps_hwt")

        s_cond_in = sem("cond_in")
        s_table_in = sem("table_in")
        s_b_in = sem("b_in")
        s_bias_in = sem("bias_in")
        s_w_in = [[sem(f"w_in{c}_{j}") for j in range(PIECES[c])] for c in range(CHUNKS)]
        s_one = sem("one_made")
        s_zeros = sem("zeros_made")
        s_warm = sem("exp_warm")
        s_mix_clear = sem("mix_clear")
        s_ident = sem("ident_made")
        s_iota = sem("iota_made")
        s_table_hi = sem("table_hi_made")
        s_table_lo = sem("table_lo_made")
        s_w_hi = sem("w_hi_made")
        s_w_lo = sem("w_lo_made")
        s_b_hi = sem("b_hi_made")
        s_b_lo = sem("b_lo_made")
        s_xt01_in = [[sem(f"xt{i}_in{h}") for h in range(2)] for i in range(2)]
        s_x01_hi = sem("x01_hi_made")
        s_x01_lo = sem("x01_lo_made")
        s_mixed01 = sem("tile0_chunk1_mixed")
        s_xt_in = [sem(f"xt_in{s}") for s in range(2)]
        s_x_in = [sem(f"x_in{s}") for s in range(2)]
        s_stored = [sem(f"stored{s}") for s in range(2)]
        s_stored_last = sem("stored_last")
        s_x_hi = sem("x_hi_ready")
        s_x_lo = sem("x_lo_ready")
        s_mix = sem("mix_ready")
        s_z = sem("z_summed")
        s_z_hi = sem("z_hi_ready")
        s_z_lo = sem("z_lo_ready")
        s_mixed0 = sem("chunk0_mixed")
        s_h = sem("h_copied")
        s_top = sem("top_ready")
        s_top_at = sem("top_at_ready")
        s_top_atf = sem("top_atf_ready")
        s_neg_top = sem("neg_top_ready")
        s_e = sem("exp_ready")
        s_e_inv = sem("e_inv_ready")
        s_w2 = sem("w2_ready")
        s_pick = sem("pick_ready")
        s_route = sem("route_ready")
        s_hw = sem("hw_ready")
        s_hwt = sem("hwt_ready")
        s_hwt_hi = sem("hwt_hi_ready")
        s_hwt_lo = sem("hwt_lo_ready")
        s_out_mm = sem("out_summed")
        s_res = sem("residual_ready")
        s_out = sem("out_ready")

        SUMMED = [(0, 0), (1, 0), (0, 1), (1, 1), (0, 2), (1, 2)]
        SPLIT = [(0, 0), (0, 1), (1, 0), (1, 1), (0, 2), (1, 2)]

        def z_summed(i, c):
            return SUMMED.index((i, c)) + 1 if isinstance(i, int) and i < 2 else i * CHUNKS + c + 1

        def z_split(i, c):
            return SPLIT.index((i, c)) + 1 if isinstance(i, int) and i < 2 else i * CHUNKS + c + 1

        def z_bank(i, c):
            return ps_z[(CHUNKS, 0, 2)[c] if isinstance(i, int) and i == 1 else c]

        def tiles(engine, step):
            with engine.Fori(1, PAIRS - 1) as g:
                for slot in range(2):
                    step(g, slot)
            for slot in range(2):
                step(PAIRS - 1, slot)

        def last(g, slot):
            return isinstance(g, int) and g == PAIRS - 1 and slot == 1

        def piece(c, j):
            return slice(j * PIECE[c], (j + 1) * PIECE[c])

        def half(h):
            return slice(h * KH, (h + 1) * KH)

        def cols(c):
            return slice(at[c], at[c] + width[c])

        block = ctx.enter_context(nc.Block())

        @block.sync
        def _(sp):
            w_src = w_t.rearrange("(k p) n -> p k n", p=P)

            def load_w(c, js):
                for j in js:
                    ks = piece(c, j)
                    sp.dma_start(w_raw[:, ks, cols(c)], w_src[:, ks, cols(c)]).then_inc(s_w_in[c][j], 16)

            def load_xt01(i, h):
                sp.dma_start(xt_sb[i][:, half(h), :], x_t[i][:, half(h), :]).then_inc(s_xt01_in[i][h], 16)

            for h in range(2):
                load_xt01(0, h)
                load_w(0, [h])
            load_w(0, range(2, PIECES[0]))
            for h in range(2):
                load_xt01(1, h)
            load_w(1, range(PIECES[1]))
            for b in range(2):
                sp.dma_start(table_raw[b * C:(b + 1) * C], cond_w).then_inc(s_table_in, 16)
            load_w(2, range(PIECES[2]))
            sp.dma_start(b_raw[:], b_t).then_inc(s_b_in, 16)
            sp.dma_start(bias[:], b_base.to_broadcast([P, O])).then_inc(s_bias_in, 16)
            for slot in range(2):
                sp.dma_start(o_sb[slot][:], x[slot * P:(slot + 1) * P, :]).then_inc(s_x_in[slot], 16)
            for slot in range(2):
                sp.wait_ge(s_x01_lo, 2 * slot + 2)
                sp.dma_start(xt_sb[slot][:], x_t[2 + slot]).then_inc(s_xt_in[slot], 16)

            def load_xt(i, slot):
                sp.wait_ge(s_x_lo, i - 3)
                sp.dma_start(xt_sb[slot][:], x_t[bass.ds(i, 1)].rearrange("a p k r -> (a p) k r"))\
                    .then_inc(s_xt_in[slot], 16)

            def load_x(i, slot, stores):
                sp.wait_ge(s_stored[slot], stores * 16)
                sp.dma_start(o_sb[slot][:], x[bass.ds(i * P, P), :]).then_inc(s_x_in[slot], 16)

            def store(i, slot):
                sp.wait_ge(s_out, i * CHUNKS + CHUNKS)
                sp.dma_start(out[bass.ds(i * P, P), :], o_sb[slot][:]).then_inc(s_stored[slot], 16)

            store(0, 0)
            load_x(2, 0, 1)
            with sp.Fori(1, PAIRS - 1) as g:
                load_xt(g * 2 + 2, 0)
                store(g * 2 - 1, 1)
                load_x(g * 2 + 1, 1, g)
                load_xt(g * 2 + 3, 1)
                store(g * 2, 0)
                load_x(g * 2 + 2, 0, g + 1)
            store(TILES - 3, 1)
            load_x(TILES - 1, 1, PAIRS - 1)
            store(TILES - 2, 0)
            for c in range(CHUNKS):
                part = slice(base_at[c], base_at[c] + BASE_COLS[c])
                sp.wait_ge(s_out, (TILES - 1) * CHUNKS + c + 1)
                sp.dma_start(out[(TILES - 1) * P:, part], o_sb[1][:, part]).then_inc(s_stored_last, 16)
            sp.wait_ge(s_stored[0], 16 * PAIRS)
            sp.wait_ge(s_stored[1], 16 * (PAIRS - 1))
            sp.wait_ge(s_stored_last, 16 * CHUNKS)

        @block.gpsimd
        def _(pool):
            for slot in range(2):
                pool.memset(mix[slot][:].bitcast(F32), 0.0).then_inc(s_mix_clear, 1)
            pool.memset(ident[:], 0.0).then_inc(s_mix_clear, 1)
            pool.iota(expert[:], [[1, E]], base=0, channel_multiplier=0,
                      allow_small_or_imprecise_dtypes=True).then_inc(s_iota, 1)
            pool.wait_ge(s_mix_clear, 3)
            pool.affine_select(out=ident[:], in_=ident[:], compare_op=ALU.not_equal, fill=1.0, base=0,
                               pattern=[[-1, P]], channel_multiplier=1).then_inc(s_ident, 1)
            pool.wait_ge(s_cond_in, 16)

            def fetch_mix(i, slot):
                for b in range(2):
                    c = pool.value_load(cond_sb[0:1, bass.ds(i * 2 + b, 1)], min_val=0, max_val=S - 1)
                    part = slice(b * C, (b + 1) * C)
                    if b == 1:
                        pool.wait_ge(s_mix, 2 * i + 1)
                    pool.tensor_copy(mix[slot][part, :, b * D:(b + 1) * D],
                                     table[part, bass.ds(c, 1), :, :].rearrange("p a h d -> p (a h) d"))\
                        .then_inc(s_mix, 1)
                pool.wait_ge(s_mix, 2 * i + 2)

            def split_x(i, slot):
                pool.wait_ge(s_x_hi, i - 1)
                pool.tensor_tensor(x_lo[slot][:], xt_sb[slot][:], x_hi[slot][:].bitcast(F32),
                                   ALU.subtract).then_inc(s_x_lo, 1)

            def residual(slot, loads):
                pool.wait_ge(s_x_in[slot], loads * 16)
                pool.tensor_tensor(o_sb[slot][:], o_sb[slot][:], bias[:], ALU.add).then_inc(s_res, 1)

            pool.wait_ge(s_ident, 1)
            pool.wait_ge(s_table_lo, 1)
            fetch_mix(0, 0)
            fetch_mix(1, 1)
            pool.wait_ge(s_bias_in, 16)
            residual(0, 1)
            split_x(2, 0)
            residual(1, 1)

            def step(g, slot):
                i = g * 2 + slot
                pool.wait_ge(s_res, i)
                pool.wait_ge(s_out_mm, (i - 1) * CHUNKS)
                fetch_mix(i, slot)
                if not last(g, slot):
                    split_x(i + 1, 1 - slot)
                residual(slot, g + 1)

            tiles(pool, step)

        @block.scalar
        def _(act):
            act.dma_start(cond_sb[:], cond).then_inc(s_cond_in, 16)
            act.wait_ge(s_one, 1)
            act.activation(e2[:], one[:], ACT.Exp).then_inc(s_warm, 1)

            def w_top(c, js):
                for j in js:
                    ks = piece(c, j)
                    act.wait_ge(s_w_in[c][j], 16)
                    act.copy(w_hi[:, ks, cols(c)], w_raw[:, ks, cols(c)]).then_inc(s_w_hi, 1)

            def x01_top(i, h):
                act.wait_ge(s_xt01_in[i][h], 16)
                act.copy(x_hi[i][:, half(h), :], xt_sb[i][:, half(h), :]).then_inc(s_x01_hi, 1)

            def x_top(slot, loads, summed):
                act.wait_ge(s_xt_in[slot], loads * 16)
                act.wait_ge(s_z, summed)
                act.copy(x_hi[slot][:], xt_sb[slot][:]).then_inc(s_x_hi, 1)

            def z_top(i, c):
                act.wait_ge(s_z, z_summed(i, c))
                act.copy(z_hi[:, cols(c)], z_bank(i, c)[:, 0:width[c]]).then_inc(s_z_hi, 1)

            def exps(i):
                act.wait_ge(s_neg_top, i + 1)
                act.activation(e2[:], top[:, 0:2], ACT.Exp, bias=neg_top[:], accum_out=e_sum[:]).then_inc(s_e, 1)

            def hwt_top(i):
                act.wait_ge(s_hwt, i + 1)
                act.copy(hwt_hi[:], ps_hwt[:, 0:P]).then_inc(s_hwt_hi, 1)

            for h in range(2):
                x01_top(0, h)
                w_top(0, [h])
            w_top(0, range(2, PIECES[0]))
            for h in range(2):
                x01_top(1, h)
            z_top(0, 0)
            w_top(1, range(PIECES[1]))
            act.wait_ge(s_table_in, 32)
            act.copy(table[:, :, 0, :], table_raw[:]).then_inc(s_table_hi, 1)
            w_top(2, range(0, 2))
            z_top(0, 1)
            w_top(2, range(2, PIECES[2]))
            act.wait_ge(s_mixed0, 1)
            z_top(1, 0)
            exps(0)
            act.wait_ge(s_b_in, 16)
            act.copy(b_hi[:], b_raw[:]).then_inc(s_b_hi, 1)
            act.wait_ge(s_mixed01, 1)
            z_top(1, 1)
            hwt_top(0)
            z_top(0, 2)
            x_top(0, 1, z_summed(0, 2))
            exps(1)
            act.wait_ge(s_out_mm, CHUNKS)
            z_top(1, 2)

            def step(g, slot):
                i = g * 2 + slot
                hwt_top(i - 1)
                act.wait_ge(s_mixed0, i)
                z_top(i, 0)
                if not last(g, slot):
                    x_top(1 - slot, g + slot, i * CHUNKS)
                act.wait_ge(s_out_mm, i * CHUNKS - 1)
                z_top(i, 1)
                exps(i)
                if last(g, slot):
                    hwt_top(i)
                act.wait_ge(s_out_mm, i * CHUNKS)
                z_top(i, 2)

            tiles(act, step)

        @block.vector
        def _(dve):
            dve.memset(zeros[:], 0.0).then_inc(s_zeros, 1)
            dve.memset(one[:], 1.0).then_inc(s_one, 1)

            def w_rest(c, js):
                for j in js:
                    ks = piece(c, j)
                    dve.wait_ge(s_w_hi, pieces_before[c] + j + 1)
                    dve.tensor_tensor(w_lo[:, ks, cols(c)], w_raw[:, ks, cols(c)],
                                      w_hi[:, ks, cols(c)].bitcast(F32), ALU.subtract).then_inc(s_w_lo, 1)

            def x01_rest(i, h):
                dve.wait_ge(s_x01_hi, 2 * i + h + 1)
                dve.tensor_tensor(x_lo[i][:, half(h), :], xt_sb[i][:, half(h), :],
                                  x_hi[i][:, half(h), :].bitcast(F32), ALU.subtract).then_inc(s_x01_lo, 1)

            def z_rest(i, c):
                dve.wait_ge(s_z_hi, z_split(i, c))
                dve.tensor_tensor(z_lo[:, cols(c)], z_bank(i, c)[:, 0:width[c]], z_hi[:, cols(c)].bitcast(F32),
                                  ALU.subtract).then_inc(s_z_lo, 1)

            def hwt_rest(i):
                dve.wait_ge(s_hwt_hi, i + 1)
                dve.tensor_tensor(hwt_lo[:], ps_hwt[:, 0:P], hwt_hi[:].bitcast(F32),
                                  ALU.subtract).then_inc(s_hwt_lo, 1)

            def output(i, slot):
                dve.wait_ge(s_res, i + 1)
                for c in range(CHUNKS):
                    dve.wait_ge(s_out_mm, i * CHUNKS + c + 1)
                    part = slice(base_at[c], base_at[c] + BASE_COLS[c])
                    dve.tensor_tensor(o_sb[slot][:, part], ps_out[c][:, 0:BASE_COLS[c]], o_sb[slot][:, part],
                                      ALU.add).then_inc(s_out, 1)

            def gate(i):
                h, logits = ps_out[0][:, H_AT:L_AT], ps_out[0][:, L_AT:L_AT + E]
                dve.wait_ge(s_mixed0, i + 1)
                dve.tensor_copy(h_sb[:], h).then_inc(s_h, 1)
                dve.max(top[:], logits).then_inc(s_top, 1)
                dve.wait_ge(s_top, i + 1)
                dve.tensor_scalar(neg_top[:], top[:, 0:1], -1.0, None, ALU.mult).then_inc(s_neg_top, 1)
                dve.max_index(top_at[:], top[:], logits).then_inc(s_top_at, 1)
                dve.wait_ge(s_top_at, i + 1)
                dve.tensor_copy(top_atf[:], top_at[:, 0:2]).then_inc(s_top_atf, 1)
                dve.wait_ge(s_e, i + 1)
                dve.reciprocal(e_inv[:], e_sum[:]).then_inc(s_e_inv, 1)
                dve.wait_ge(s_e_inv, i + 1)
                dve.tensor_scalar(w2[:], e2[:], e_inv[:], None, ALU.mult).then_inc(s_w2, 1)
                dve.wait_ge(s_top_atf, i + 1)
                dve.wait_ge(s_w2, i + 1)
                for j in range(2):
                    dve.tensor_scalar(pick[:, j, :], expert[:], top_atf[:, j:j + 1], w2[:, j:j + 1],
                                      ALU.is_equal, ALU.mult).then_inc(s_pick, 1)
                dve.wait_ge(s_pick, 2 * i + 2)
                dve.tensor_tensor(route[:], pick[:, 0, :], pick[:, 1, :], ALU.add).then_inc(s_route, 1)
                dve.wait_ge(s_h, i + 1)
                dve.wait_ge(s_route, i + 1)
                dve.tensor_tensor(hw[:].rearrange("p (e r) -> p e r", e=E), h_sb[:].rearrange("p (e r) -> p e r", e=E),
                                  route[:].unsqueeze(2).to_broadcast([P, E, R]), ALU.mult).then_inc(s_hw, 1)

            for h in range(2):
                x01_rest(0, h)
                w_rest(0, [h])
            w_rest(0, range(2, PIECES[0]))
            for h in range(2):
                x01_rest(1, h)
            z_rest(0, 0)
            w_rest(1, range(PIECES[1]))
            dve.wait_ge(s_table_hi, 1)
            dve.tensor_tensor(table[:, :, 1, :], table_raw[:], table[:, :, 0, :].bitcast(F32),
                              ALU.subtract).then_inc(s_table_lo, 1)
            w_rest(2, range(0, 2))
            z_rest(0, 1)
            w_rest(2, range(2, PIECES[2]))
            z_rest(1, 0)
            dve.wait_ge(s_iota, 1)
            gate(0)
            dve.wait_ge(s_b_hi, 1)
            dve.tensor_tensor(b_lo[:], b_raw[:], b_hi[:].bitcast(F32), ALU.subtract).then_inc(s_b_lo, 1)
            z_rest(1, 1)
            hwt_rest(0)
            z_rest(0, 2)
            output(0, 0)
            gate(1)
            z_rest(1, 2)

            def step(g, slot):
                i = g * 2 + slot
                hwt_rest(i - 1)
                z_rest(i, 0)
                output(i - 1, 1 - slot)
                z_rest(i, 1)
                gate(i)
                if last(g, slot):
                    hwt_rest(i)
                z_rest(i, 2)

            tiles(dve, step)
            output(TILES - 1, 1)

        @block.tensor
        def _(pe):
            def dense(i, slot, c, k):
                for q, (a, w) in enumerate(((x_hi, w_hi), (x_hi, w_lo), (x_lo, w_hi))):
                    mm = pe.matmul(z_bank(i, c)[:, 0:width[c]], a[slot][:, k, :], w[:, k, cols(c)],
                                   start=(k == 0 and q == 0), stop=(k == KT - 1 and q == 2))
                if k == KT - 1:
                    mm.then_inc(s_z, 1)

            def mix_chunk(i, slot, c):
                pe.wait_ge(s_z_lo, z_split(i, c))
                if c == 0:
                    pe.wait_ge(s_mix, 2 * i + 2)
                if not (isinstance(i, int) and i == 0):
                    pe.wait_ge(s_out, (i - 1) * CHUNKS + c + 1)
                for q, (m, z) in enumerate(((0, z_hi), (0, z_lo), (1, z_hi))):
                    mm = pe.matmul(ps_out[c][:, 0:width[c]], mix[slot][:, m, :], z[:, cols(c)],
                                   start=(q == 0), stop=(q == 2))
                if c == 0:
                    mm.then_inc(s_mixed0, 1)
                return mm

            def turn_hw(i):
                pe.wait_ge(s_hw, i + 1)
                pe.transpose(ps_hwt[:, 0:P], hw[:], ident[:]).then_inc(s_hwt, 1)

            def lora(i, c):
                if c == 0:
                    pe.wait_ge(s_hwt_lo, i + 1)
                part = slice(base_at[c], base_at[c] + BASE_COLS[c])
                for q, (h, b) in enumerate(((hwt_hi, b_hi), (hwt_hi, b_lo), (hwt_lo, b_hi))):
                    mm = pe.matmul(ps_out[c][:, 0:BASE_COLS[c]], h[:], b[:, part], start=False,
                                   stop=(q == 2), skip_group_check=True)
                mm.then_inc(s_out_mm, 1)

            def finish(i, slot):
                mix_chunk(i, slot, 1)
                lora(i, 0)
                lora(i, 1)
                mix_chunk(i, slot, 2)
                lora(i, 2)

            def dense01(i, c, ks=range(KT)):
                for k in ks:
                    if c == 0 and k % KH == 0:
                        pe.wait_ge(s_x01_lo, 2 * i + k // KH + 1)
                    if i == 0 and k % PIECE[c] == 0:
                        pe.wait_ge(s_w_lo, pieces_before[c] + k // PIECE[c] + 1)
                    dense(i, i, c, k)

            pe.wait_ge(s_zeros, 1)
            for _ in range(WARM_UP):
                pe.matmul(ps_hwt[:], zeros[:, 0:P], zeros[:], start=True, stop=True)

            dense01(0, 0)
            dense01(1, 0)
            dense01(0, 1)
            pe.wait_ge(s_z_lo, z_split(0, 0))
            dense01(1, 1, range(KH))
            mix_chunk(0, 0, 0)
            dense01(1, 1, range(KH, KT))
            mix_chunk(0, 0, 1).then_inc(s_mixed01, 1)
            dense01(0, 2, range(KH))
            pe.wait_ge(s_ident, 1)
            turn_hw(0)
            dense01(0, 2, range(KH, KT))
            pe.wait_ge(s_b_lo, 1)
            lora(0, 0)
            lora(0, 1)
            mix_chunk(0, 0, 2)
            lora(0, 2)
            pe.wait_ge(s_z_lo, z_split(0, 2))
            dense01(1, 2, range(KH))
            mix_chunk(1, 1, 0)
            dense01(1, 2, range(KH, KT))

            def step(g, slot):
                i = g * 2 + slot
                pe.wait_ge(s_x_lo, i - 1)
                pe.wait_ge(s_z_lo, i * CHUNKS - 2)
                for k in range(KH):
                    dense(i, slot, 0, k)
                turn_hw(i - 1)
                for k in range(KH, KT):
                    dense(i, slot, 0, k)
                finish(i - 1, 1 - slot)
                pe.wait_ge(s_z_lo, i * CHUNKS - 1)
                for k in range(KT):
                    dense(i, slot, 1, k)
                mix_chunk(i, slot, 0)
                pe.wait_ge(s_z_lo, i * CHUNKS)
                for k in range(KT):
                    if last(g, slot) and k == KT - 1:
                        turn_hw(i)
                    dense(i, slot, 2, k)

            tiles(pe, step)
            finish(TILES - 1, 1)


def kernel(x, itok_B_0_15, L0_cond_weights, L0_ffn_W_base, L0_ffn_b_base, L0_ffn_W_gate, L0_ffn_A, L0_ffn_B):
    import numpy as np
    import concourse.bacc as bacc
    from concourse.bass_utils import run_bass_kernel_spmd

    batches, channels, t = x.shape
    experts, rank, _ = L0_ffn_A.shape
    o = L0_ffn_W_base.shape[0]
    rows = np.reshape(x, (batches * channels, t))
    n0 = BASE_COLS[0]
    w_rows = [L0_ffn_W_base[:n0], np.reshape(L0_ffn_A, (experts * rank, t)), L0_ffn_W_gate, L0_ffn_W_base[n0:]]
    arrays = {
        "x": rows,
        "x_t": np.transpose(np.reshape(rows, (-1, P, t // P, P)), (0, 3, 2, 1)),
        "cond": np.reshape(itok_B_0_15, (1, batches)),
        "cond_w": np.transpose(L0_cond_weights, (1, 0, 2)),
        "w_t": np.transpose(np.concatenate(w_rows)),
        "b_t": np.reshape(np.transpose(L0_ffn_B, (0, 2, 1)), (experts * rank, o)),
        "b_base": np.reshape(L0_ffn_b_base, (1, o)),
    }
    nc = bacc.Bacc("TRN2", target_bir_lowering=False, num_devices=1)
    ins, args = {}, []
    for name, a in arrays.items():
        a = np.ascontiguousarray(a)
        ins[f"in_{name}"] = a
        args.append(nc.dram_tensor(f"in_{name}", a.shape, mybir.dt.from_np(a.dtype), kind="ExternalInput").ap())
    out = nc.dram_tensor("out_x", (batches * channels, o), F32, kind="ExternalOutput").ap()
    adaln_ffn(nc, *args, out)
    r = run_bass_kernel_spmd(nc, [ins], core_ids=[0])
    return np.reshape(r.results[0]["out_x"], (batches, channels, o))
```
